# Optimizing a Trainium2 kernel written in Bass

```python
import numpy as np
import jax
import jax.numpy as jnp

def _softmax(x, axis=-1):
    return jax.nn.softmax(x, axis=axis)

def _gelu(x):
    return jax.nn.gelu(x, approximate=True)

def _silu(x):
    return jax.nn.silu(x)

def _sigmoid(x):
    return jax.nn.sigmoid(x)

def _layernorm(x, axis=-1, eps=1e-05):
    m = jnp.mean(x, axis=axis, keepdims=True)
    v = jnp.var(x, axis=axis, keepdims=True)
    return (x - m) / jnp.sqrt(v + eps)

def _scatter_add(tgt, idx, src, axis=0):
    return tgt.at[idx].add(src)

def _segment_sum(src, seg, n):
    return jax.ops.segment_sum(src, seg, n)
kernel_name = 'mk_gnn_preln_d4_gnn_r32_bfa83d'

def setup_inputs(seed: int=0):
    np.random.seed(seed)
    _w = jnp.asarray

    def _rec_inputs():
        import jax
        import jax.numpy as jnp
        _gk = jax.random.key(seed)
        x = -0.0005121 + 1.001 * jax.random.normal(jax.random.fold_in(_gk, 1), (3125, 32), jnp.float32)
        _s = jax.random.randint(jax.random.fold_in(_gk, 2), (50000,), 0, 3125, jnp.int32)
        _d = jax.random.randint(jax.random.fold_in(_gk, 3), (50000,), 0, 3125, jnp.int32)
        _loop = jnp.arange(3125, dtype=jnp.int32)
        src = jnp.concatenate([_s, _d, _loop])
        dst = jnp.concatenate([_d, _s, _loop])
        _o = jnp.argsort(dst, stable=True)
        src = src[_o]
        dst = dst[_o]
        edge_attr_32 = 0.000216709 + 1.00012 * jax.random.normal(jax.random.fold_in(_gk, 12), (103125, 32), jnp.float32)
        edge_attr_4 = 0.000714719 + 1.00021 * jax.random.normal(jax.random.fold_in(_gk, 13), (103125, 4), jnp.float32)
        edge_type_8 = jax.random.randint(jax.random.fold_in(_gk, 15), (103125,), 0, 8, jnp.int32)
        edge_weight = jax.random.uniform(jax.random.fold_in(_gk, 16), (103125,), jnp.float32, 0.0, 1)
        return (x, src, dst, edge_attr_32, edge_attr_4, edge_type_8, edge_weight)
    x, src, dst, edge_attr_32, edge_attr_4, edge_type_8, edge_weight = _rec_inputs()

    def _L0_gnn_setup():
        import jax, jax.numpy as jnp
        import numpy as np
        MUL = 8
        N_NODES = 3125
        N_EDGES = 25000
        EDGE_DIM = 32
        MLP_DIM = 64
        W_NUMEL = 4 * MUL * MUL
        ALPHA = 0.25
        C110 = 1.0 / np.sqrt(3.0)
        SI_SCALE = 1.0 / np.sqrt(MUL)
        key = jax.random.key(seed)
        ks = jax.random.split(key, 10)
        node_attr = jax.random.normal(ks[0], (N_NODES, 4 * MUL), dtype=jnp.float32)
        edge_index = jax.random.randint(ks[1], (2, N_EDGES), 0, N_NODES, dtype=jnp.int64)
        edge_sh = jax.random.normal(ks[2], (N_EDGES, 4), dtype=jnp.float32)
        edge_feat = jax.random.normal(ks[3], (N_EDGES, EDGE_DIM), dtype=jnp.float32)
        W1 = jax.random.normal(ks[4], (EDGE_DIM, MLP_DIM), dtype=jnp.float32) / np.sqrt(EDGE_DIM)
        b1 = jnp.zeros((MLP_DIM,), dtype=jnp.float32)
        W2 = jax.random.normal(ks[5], (MLP_DIM, W_NUMEL), dtype=jnp.float32) / np.sqrt(MLP_DIM)
        b2 = jnp.zeros((W_NUMEL,), dtype=jnp.float32)
        si_w0 = jax.random.normal(ks[6], (MUL, MUL), dtype=jnp.float32)
        si_w1 = jax.random.normal(ks[7], (MUL, MUL), dtype=jnp.float32)
        return {'node_attr': node_attr, 'edge_index': edge_index, 'edge_sh': edge_sh, 'edge_feat': edge_feat, 'W1': W1, 'b1': b1, 'W2': W2, 'b2': b2, 'si_w0': si_w0, 'si_w1': si_w1}
    _L0_gnn_all = _L0_gnn_setup()
    _L0_gnn_in = {k: v for k, v in _L0_gnn_all.items() if k in ('W1', 'b1', 'W2', 'b2', 'si_w0', 'si_w1')}
    del _L0_gnn_all

    def _L1_gnn_setup():
        import jax, jax.numpy as jnp
        import numpy as np
        N_NODES = 3125
        N_EDGES = 50000
        LATENT_DIM = 32
        NUM_LAYERS = 3
        key = jax.random.key(seed)
        k_x, k_e = jax.random.split(key)
        x = jax.random.normal(k_x, (N_NODES, LATENT_DIM), dtype=jnp.float32)
        edge_index = jax.random.randint(k_e, (2, N_EDGES), 0, N_NODES, dtype=jnp.int64)
        return {'x': x, 'edge_index': edge_index, 'num_layers': NUM_LAYERS}
    _L1_gnn_all = _L1_gnn_setup()
    _L1_gnn_in = {k: v for k, v in _L1_gnn_all.items() if k in ()}
    del _L1_gnn_all

    def _L2_gnn_setup():
        import jax, jax.numpy as jnp
        import numpy as np
        N_NODES = 3125
        N_EDGES = 50000
        N_FEAT = 32
        key = jax.random.key(seed)
        k1, k2, k3, k4 = jax.random.split(key, 4)
        u = jax.random.normal(k1, (N_NODES, N_FEAT), dtype=jnp.float32)
        weights = jax.random.uniform(k2, (N_EDGES,), dtype=jnp.float32)
        row = jax.random.randint(k3, (N_EDGES,), 0, N_NODES)
        col = jax.random.randint(k4, (N_EDGES,), 0, N_NODES)
        edge_index = jnp.stack([row, col]).astype(jnp.int64)
        return {'u': u, 'weights': weights, 'edge_index': edge_index}
    _L2_gnn_all = _L2_gnn_setup()
    _L2_gnn_in = {k: v for k, v in _L2_gnn_all.items() if k in ()}
    del _L2_gnn_all

    def _L3_gnn_setup():
        import jax, jax.numpy as jnp
        import numpy as np
        N = 50000
        E = 25000
        IN = 32
        H = 32
        OUT = 32
        R = 8
        Q = 4

        def _xavier(key, shape):
            gain = 5.0 / 3.0
            fan_in, fan_out = (shape[-2], shape[-1])
            limit = gain * np.sqrt(6.0 / (fan_in + fan_out))
            return jax.random.uniform(key, shape, jnp.float32, -limit, limit)

        def _layer(h, W, b, src, dst, etypes, tv):
            hp = jnp.einsum('ni,rqio->nrqo', h, W)
            msg = jnp.einsum('eq,eqo->eo', tv, hp[src, etypes])
            msg = msg + jnp.einsum('eq,eqo->eo', tv, b[etypes])
            return jax.ops.segment_sum(msg, dst, num_segments=h.shape[0])
        key = jax.random.key(seed)
        ks = jax.random.split(key, 7)
        feat = jax.random.normal(ks[0], (N, IN), jnp.float32)
        src = jax.random.randint(ks[1], (E,), 0, N, dtype=jnp.int32)
        dst = jax.random.randint(ks[2], (E,), 0, N, dtype=jnp.int32)
        etypes = jax.random.randint(ks[3], (E,), 0, R, dtype=jnp.int32)
        truth_value = jax.random.uniform(ks[4], (E, Q), jnp.float32)
        W1 = _xavier(ks[5], (R, Q, IN, H))
        W2 = _xavier(ks[6], (R, Q, H, OUT))
        b1 = jnp.zeros((R, Q, H), jnp.float32)
        b2 = jnp.zeros((R, Q, OUT), jnp.float32)
        return dict(feat=feat, truth_value=truth_value, W1=W1, b1=b1, W2=W2, b2=b2, src=src, dst=dst, etypes=etypes)
    _L3_gnn_all = _L3_gnn_setup()
    _L3_gnn_in = {k: v for k, v in _L3_gnn_all.items() if k in ('W1', 'b1', 'W2', 'b2')}
    del _L3_gnn_all
    return {'x': x, 'src': src, 'dst': dst, 'edge_attr_32': edge_attr_32, 'edge_attr_4': edge_attr_4, 'edge_type_8': edge_type_8, 'edge_weight': edge_weight, 'L0_gnn_W1': _L0_gnn_in['W1'], 'L0_gnn_b1': _L0_gnn_in['b1'], 'L0_gnn_W2': _L0_gnn_in['W2'], 'L0_gnn_b2': _L0_gnn_in['b2'], 'L0_gnn_si_w0': _L0_gnn_in['si_w0'], 'L0_gnn_si_w1': _L0_gnn_in['si_w1'], 'L3_gnn_W1': _L3_gnn_in['W1'], 'L3_gnn_b1': _L3_gnn_in['b1'], 'L3_gnn_W2': _L3_gnn_in['W2'], 'L3_gnn_b2': _L3_gnn_in['b2']}

def reference(x, src, dst, edge_attr_32, edge_attr_4, edge_type_8, edge_weight, L0_gnn_W1, L0_gnn_b1, L0_gnn_W2, L0_gnn_b2, L0_gnn_si_w0, L0_gnn_si_w1, L3_gnn_W1, L3_gnn_b1, L3_gnn_W2, L3_gnn_b2):
    import jax
    import jax.numpy as jnp

    def _L0_gnn_ref(node_attr, edge_index, edge_sh, edge_feat, W1, b1, W2, b2, si_w0, si_w1):
        import jax, jax.numpy as jnp
        import numpy as np
        MUL = 8
        N_NODES = 3125
        N_EDGES = 25000
        EDGE_DIM = 32
        MLP_DIM = 64
        W_NUMEL = 4 * MUL * MUL
        ALPHA = 0.25
        C110 = 1.0 / np.sqrt(3.0)
        SI_SCALE = 1.0 / np.sqrt(MUL)
        n = node_attr.shape[0]
        e = edge_sh.shape[0]
        h = jax.nn.relu(edge_feat @ W1 + b1)
        w = (h @ W2 + b2).reshape(e, 4, MUL, MUL)
        w_000, w_011, w_101, w_110 = (w[:, 0], w[:, 1], w[:, 2], w[:, 3])
        s = node_attr[:, :MUL]
        v = node_attr[:, MUL:].reshape(n, MUL, 3)
        src, dst = (edge_index[0], edge_index[1])
        s_e = s[src]
        v_e = v[src]
        sh0 = edge_sh[:, 0]
        sh1 = edge_sh[:, 1:4]
        m0 = ALPHA * (jnp.einsum('ei,eio->eo', s_e * sh0[:, None], w_000) + C110 * jnp.einsum('eim,em,eio->eo', v_e, sh1, w_110))
        m1 = ALPHA * (jnp.einsum('ei,em,eio->eom', s_e, sh1, w_011) + jnp.einsum('eim,eio->eom', v_e * sh0[:, None, None], w_101))
        out0 = jax.ops.segment_sum(m0, dst, num_segments=n)
        out1 = jax.ops.segment_sum(m1.reshape(e, MUL * 3), dst, num_segments=n).reshape(n, MUL, 3)
        out0 = out0 + SI_SCALE * (s @ si_w0)
        out1 = out1 + SI_SCALE * jnp.einsum('nim,io->nom', v, si_w1)
        return jnp.concatenate([out0, out1.reshape(n, MUL * 3)], axis=-1)

    def _L1_gnn_ref(x, edge_index, num_layers):
        import jax, jax.numpy as jnp
        import numpy as np
        N_NODES = 3125
        N_EDGES = 50000
        LATENT_DIM = 32
        NUM_LAYERS = 3
        N = x.shape[0]
        src = edge_index[0]
        dst = edge_index[1]
        cnt = jax.ops.segment_sum(jnp.ones((edge_index.shape[1],), x.dtype), dst, num_segments=N)
        denom = jnp.maximum(cnt, 1.0)[:, None]
        scale = 1.0 / (num_layers + 1)
        final = x * scale
        for _ in range(num_layers):
            summed = jax.ops.segment_sum(x[src], dst, num_segments=N)
            x = summed / denom
            final = final + x * scale
        return final

    def _L2_gnn_ref(u, weights, edge_index):
        import jax, jax.numpy as jnp
        import numpy as np
        N_NODES = 3125
        N_EDGES = 50000
        N_FEAT = 32
        row, col = (edge_index[0], edge_index[1])
        diff = u[col] - u[row]
        weighted_diff = weights[:, None] * diff
        laplacian = jax.ops.segment_sum(weighted_diff, row, num_segments=u.shape[0])
        return laplacian

    def _L3_gnn_ref(feat, truth_value, W1, b1, W2, b2, src, dst, etypes):
        import jax, jax.numpy as jnp
        import numpy as np
        N = 50000
        E = 25000
        IN = 32
        H = 32
        OUT = 32
        R = 8
        Q = 4

        def _xavier(key, shape):
            gain = 5.0 / 3.0
            fan_in, fan_out = (shape[-2], shape[-1])
            limit = gain * np.sqrt(6.0 / (fan_in + fan_out))
            return jax.random.uniform(key, shape, jnp.float32, -limit, limit)

        def _layer(h, W, b, src, dst, etypes, tv):
            hp = jnp.einsum('ni,rqio->nrqo', h, W)
            msg = jnp.einsum('eq,eqo->eo', tv, hp[src, etypes])
            msg = msg + jnp.einsum('eq,eqo->eo', tv, b[etypes])
            return jax.ops.segment_sum(msg, dst, num_segments=h.shape[0])
        x = jnp.tanh(_layer(feat, W1, b1, src, dst, etypes, truth_value))
        return _layer(x, W2, b2, src, dst, etypes, truth_value)
    edge_index = jnp.stack([src, dst])
    h = jnp.maximum(_layernorm(x, axis=-1), 0.0)
    x = x + _L0_gnn_ref(h, edge_index, edge_attr_4, edge_attr_32, L0_gnn_W1, L0_gnn_b1, L0_gnn_W2, L0_gnn_b2, L0_gnn_si_w0, L0_gnn_si_w1)
    h = jnp.maximum(_layernorm(x, axis=-1), 0.0)
    x = x + _L1_gnn_ref(h, edge_index, 3)
    h = jnp.maximum(_layernorm(x, axis=-1), 0.0)
    x = x + _L2_gnn_ref(h, edge_weight, edge_index)
    h = jnp.maximum(_layernorm(x, axis=-1), 0.0)
    x = x + _L3_gnn_ref(h, edge_attr_4, L3_gnn_W1, L3_gnn_b1, L3_gnn_W2, L3_gnn_b2, src, dst, edge_type_8)
    return x

_drawn_inputs = setup_inputs


def setup_inputs(seed=0):
    import zlib

    import numpy as np

    out = dict(_drawn_inputs(seed))
    spreads = {'L0_gnn_b1': (0.0, 0.1),
     'L0_gnn_b2': (0.0, 0.1),
     'L3_gnn_b1': (0.0, 0.1),
     'L3_gnn_b2': (0.0, 0.1)}
    factors = {}
    for name, (base, spread) in spreads.items():
        noise = np.random.default_rng([zlib.crc32(name.encode()), seed]).standard_normal(out[name].shape)
        drawn = base * np.exp(spread * noise) if base else spread * noise
        out[name] = jnp.asarray(drawn.astype(out[name].dtype))
    for name, factor in factors.items():
        out[name] = (out[name] * factor).astype(out[name].dtype)
    return out
```

```python
from contextlib import ExitStack

import numpy as np

import concourse.bass as bass
from concourse import mybir

F32 = mybir.dt.float32
I32 = mybir.dt.int32
ALU = mybir.AluOpType
ACT = mybir.ActivationFunctionType
AX_X = mybir.AxisListType.X

P = 128
N_NODES, FEAT = 3125, 32
N_EDGES = 103125
BLOCKS = -(-N_NODES // P)
NODES = BLOCKS * P
PAD_NODE = NODES - 1
CHUNK_TILES = 4
SLOTS = 4
TURNS = -(-N_EDGES // (P * CHUNK_TILES * SLOTS))
CHUNKS = TURNS * SLOTS
TILES = CHUNKS * CHUNK_TILES
EDGES = TILES * P
CHUNK_EDGES = CHUNK_TILES * P
GROUP_TILES = 2 * CHUNK_TILES
GROUPS = TILES // GROUP_TILES
MUL = 8
EDGE_DIM, MLP_DIM, PATHS = 32, 64, 4
RELS, Q = 8, 4
ROW = Q * FEAT
LANES = 4
GROUP_P = 112
GROUP_COLS = 7
LAP_GROUPS = GROUP_P * GROUP_COLS
LAP_HALF = LAP_GROUPS // 2
ALPHA = 0.25
C110 = 1.0 / np.sqrt(3.0)
SI_SCALE = 1.0 / np.sqrt(MUL)
EPS = 1e-5
HOPS = 3
ACC_STEP = 64


def build(nc, x, dst_rows, src_groups, dst_groups, type_groups, src_tiles, dst_tiles, weight_tiles,
          sh_tiles, edge_feat, w1, b1, w2, self_w, rel_w1, rel_w2, out):
    with ExitStack() as ctx:
        def sb(name, shape, dt=F32):
            return ctx.enter_context(nc.sbuf_tensor(name, shape, dt))

        def sem(name):
            return ctx.enter_context(nc.semaphore(name))

        node_table = nc.dram_tensor("node_table", [NODES, FEAT], F32, kind="Internal").ap()
        rel_table = nc.dram_tensor("rel_table", [NODES * RELS, ROW], F32, kind="Internal").ap()
        rel_groups = nc.dram_tensor("rel_groups", [GROUPS, P, GROUP_TILES], I32, kind="Internal").ap()
        range_rows = nc.dram_tensor("range_rows", [2, CHUNKS], F32, kind="Internal").ap()
        lap_rows = nc.dram_tensor("lap_rows", [NODES, FEAT], F32, kind="Internal").ap()

        msgs = sb("msgs", [P, TILES, FEAT])
        flat = msgs[:].rearrange("p t f -> p (t f)")
        gathered = sb("gathered", [P, SLOTS, CHUNK_TILES, ROW])
        index = sb("index", [P, 2, GROUP_TILES], I32)
        neg_dst = sb("neg_dst", [P, TILES])
        src_group = sb("src_group", [P, TILES])
        src_low = sb("src_low", [P, TILES])
        src_block = sb("src_block", [P, TILES])
        weight = sb("weight", [P, TILES])
        sh = sb("sh", [P, TILES, 4])
        node_iota = sb("node_iota", [P, NODES])
        onehot = sb("onehot", [P, CHUNK_TILES, P])
        distance = sb("distance", [P, CHUNK_TILES, P])
        coef = sb("coef", [P, CHUNK_TILES, 6, MUL])
        dots = sb("dots", [P, CHUNK_TILES, MUL, 3])
        prods = sb("prods", [P, CHUNK_TILES, 6, MUL, MUL])
        sums = sb("sums", [P, CHUNK_TILES, 6, MUL])
        scaled_sh = sb("scaled_sh", [P, CHUNK_TILES, 8])
        spread = sb("spread", [P, CHUNK_TILES, MUL, 3])
        feat_in = sb("feat_in", [EDGE_DIM, 2, CHUNK_EDGES])
        hidden = sb("hidden", [MLP_DIM + 1, 2, CHUNK_EDGES])
        w1_sb = sb("w1_sb", [EDGE_DIM, MLP_DIM])
        b1_sb = sb("b1_sb", [MLP_DIM, 1])
        w2_sb = sb("w2_sb", [MLP_DIM + 1, PATHS * MUL * MUL])
        self_sb = sb("self_sb", [FEAT, FEAT])
        ident = sb("ident", [P, P])
        diag = sb("diag", [P, P])
        below = sb("below", [P, BLOCKS])
        span_rows = sb("span_rows", [1, 3, BLOCKS])
        zeros = sb("zeros", [P, P])
        ones = sb("ones", [P, 1])
        block_start = sb("block_start", [P, 1])
        spans = sb("spans", [1, 96], I32)
        xs = sb("xs", [P, BLOCKS, FEAT])
        hs = sb("hs", [P, BLOCKS, FEAT])
        tmp = sb("tmp", [P, BLOCKS, FEAT])
        final = sb("final", [P, BLOCKS, FEAT])
        stat = sb("stat", [P, 6, BLOCKS])
        mean_scale = sb("mean_scale", [P, BLOCKS])
        out_weight = sb("out_weight", [P, BLOCKS])

        node_t = flat[0:FEAT + 1, 0:NODES]
        rel_w = flat[0:FEAT + 1, NODES:NODES + 2 * RELS * ROW].rearrange("p (l c) -> p l c", l=2)
        rel_rows = flat[:, 6000:6000 + 2 * RELS * ROW].rearrange("p (s c) -> p s c", s=2)
        setup_src = flat[:, 10000:10000 + TILES].bitcast(I32)
        setup_tmp = flat[:, 11000:11000 + TILES].bitcast(I32)
        setup_dst = flat[:, 12000:12000 + TILES].bitcast(I32)
        setup_rows = flat[0:CHUNKS // 2, 13000:13000 + 2 * CHUNK_EDGES].bitcast(I32)
        row_range = flat[0:CHUNKS // 2, 15000:15004].rearrange("p (m k) -> p m k", m=2)
        ranges = flat[0:BLOCKS, 15100:15100 + 2 * CHUNKS].rearrange("p (m c) -> p m c", m=2)
        range_tmp = flat[0:BLOCKS, 15600:15600 + 3 * CHUNKS].rearrange("p (m c) -> p m c", m=3)
        bounds = flat[0:BLOCKS, 16300:16308]
        rel_index = flat[0:GROUPS, 17000:17000 + 3 * P * GROUP_TILES].bitcast(I32).rearrange(
            "p (m c) -> p m c", m=3)
        lane_weight = flat[:, 0:TILES * LANES].rearrange("p (t l) -> p t l", l=LANES)
        group_hot = flat[:, 4000:4000 + 4 * LAP_GROUPS].rearrange("p (s c) -> p s c", s=4)
        lap_lhs = flat[:, 8000:8000 + 2 * CHUNK_TILES * P].rearrange("p (s t c) -> p s t c", s=2, t=CHUNK_TILES)
        low_hot = flat[:, 10000:10000 + 4 * P].rearrange("p (s c) -> p s c", s=4)
        block_hot = flat[:, 11000:11000 + 4 * BLOCKS].rearrange("p (s c) -> p s c", s=4)
        lap_t = flat[:, 12000:12000 + LAP_GROUPS]
        lap_nodes = flat[0:GROUP_P, 13000:13000 + GROUP_COLS * P]
        lane_tmp = flat[:, 14000:14000 + TILES].bitcast(I32)
        lane_src = flat[:, 15000:15000 + TILES].bitcast(I32)
        lane = flat[:, 16000:16000 + TILES]

        acc = ctx.enter_context(nc.psum_tensor("acc", [P, 4, 512], F32))
        work = ctx.enter_context(nc.psum_tensor("work", [P, 4, 512], F32))
        acc_flat = acc[:].rearrange("p b c -> p (b c)")
        acc_blocks = acc_flat[:, 0:BLOCKS * ACC_STEP].rearrange("p (b c) -> p b c", c=ACC_STEP)
        work_flat = work[:].rearrange("p b c -> p (b c)")

        x_loaded, params_loaded, rel_w_loaded = sem("x_loaded"), sem("params_loaded"), sem("rel_w_loaded")
        rows_loaded, groups_loaded, tiles_loaded = sem("rows_loaded"), sem("groups_loaded"), sem("tiles_loaded")
        lane_loaded = sem("lane_loaded")
        iota_done, consts_done = sem("iota_done"), sem("consts_done")
        vec = sem("vec")
        row_range_ready, row_range_stored, ranges_loaded = sem("row_range_ready"), sem("row_range_stored"), sem("ranges_loaded")
        bounds_ready, bounds_turned, spans_ready = sem("bounds_ready"), sem("bounds_turned"), sem("spans_ready")
        rel_index_ready, rel_index_stored = sem("rel_index_ready"), sem("rel_index_stored")
        setup_done = sem("setup_done")
        var_ready, std_ready = sem("var_ready"), sem("std_ready")
        table_ready, table_stored = sem("table_ready"), sem("table_stored")
        vec_self_read = sem("vec_self_read")
        h_turned, h_turned_copied, self_done = sem("h_turned"), sem("h_turned_copied"), sem("self_done")
        feat_loaded = [sem(f"feat_loaded{s}") for s in range(2)]
        hidden_psum, hidden_ready = sem("hidden_psum"), sem("hidden_ready")
        mix_ready, mix_read, conv_step = sem("mix_ready"), sem("mix_read"), sem("conv_step")
        rel_psum = [sem(f"rel_psum{s}") for s in range(2)]
        rel_copied = [sem(f"rel_copied{s}") for s in range(2)]
        rel_stored = [sem(f"rel_stored{s}") for s in range(2)]
        rel_in, rel_in_copied = sem("rel_in"), sem("rel_in_copied")
        rel_prod = [sem("rel_prod1"), sem("rel_prod2")]
        tanh_in, tanh_done = sem("tanh_in"), sem("tanh_done")
        lap_zeroed, lap_msg, lap_tile_ready, lap_tile_done = sem("lap_zeroed"), sem("lap_msg"), sem("lap_tile_ready"), sem("lap_tile_done")
        lap_summed, lap_copied, lap_turned, lap_out = sem("lap_summed"), sem("lap_copied"), sem("lap_turned"), sem("lap_out")
        lap_stored, lap_loaded = sem("lap_stored"), sem("lap_loaded")
        out_ready, out_stored = sem("out_ready"), sem("out_stored")

        class Pass:

            def __init__(self, name, groups, table, row, vector_tiles=0):
                self.groups, self.table, self.row = groups, table, row
                self.vector_tiles = vector_tiles
                self.index_ready = [sem(f"index_ready{g}_{name}") for g in range(2)]
                self.rows_ready = [sem(f"rows_ready{k}_{name}") for k in range(SLOTS)]
                self.slots_taken = sem(f"slots_taken_{name}")
                self.msg_ready = sem(f"msg_ready_{name}")
                self.dist_ready = sem(f"dist_ready_{name}")
                self.vector_hots = sem(f"vector_hots_{name}") if vector_tiles else None
                self.scalar_hots = sem(f"scalar_hots_{name}")
                self.hot_free = sem(f"hot_free_{name}")
                self.blocks_done = sem(f"blocks_done_{name}")

        conv = Pass("conv", src_groups, node_table, FEAT, vector_tiles=3)
        hops = [Pass(f"hop{h}", src_groups, node_table, FEAT) for h in range(HOPS)]
        lap = Pass("lap", dst_groups, node_table, FEAT)
        rels = [Pass(f"rel{n}", rel_groups, rel_table, ROW) for n in range(2)]

        tabled = node_table.rearrange("(b p) f -> p b f", p=P)

        def wait_from(eng, sem_, value):
            if not isinstance(value, int) or value > 0:
                eng.wait_ge(sem_, value)

        def turns(eng, body):
            body(0)
            with eng.Fori(1, TURNS) as i:
                body(i)

        def each_step(eng, open_block, step, close_block):
            with eng.Fori(0, BLOCKS) as b:
                first = eng.value_load(spans[0:1, bass.ds(b, 1)], min_val=0, max_val=CHUNKS - 1)
                end = eng.value_load(spans[0:1, bass.ds(b + 32, 1)], min_val=1, max_val=CHUNKS)
                lead = eng.value_load(spans[0:1, bass.ds(b + 64, 1)], min_val=1, max_val=(BLOCKS + 1) * CHUNKS)
                open_block(b)
                with eng.Fori(first, end) as chunk:
                    step(b, chunk + lead, chunk)
                close_block(b)

        block = ctx.enter_context(nc.Block())

        @block.sync
        def _(sp):
            sp.dma_start(xs[:], x.rearrange("(b p) f -> p b f", p=P)).then_inc(x_loaded, 16)
            sp.dma_start(setup_rows, dst_rows.rearrange("(p k) e -> p (k e)", k=2)).then_inc(rows_loaded, 16)
            for to, what in ((w1_sb[:], w1), (b1_sb[:], b1), (w2_sb[:], w2), (self_sb[:], self_w)):
                sp.dma_start(to, what).then_inc(params_loaded, 16)
            for to, what in ((setup_src, src_tiles), (setup_dst, dst_tiles), (weight[:], weight_tiles),
                             (sh[:], sh_tiles)):
                sp.dma_start(to, what).then_inc(tiles_loaded, 16)
            for m, what in ((0, src_groups), (1, type_groups)):
                sp.dma_start(rel_index[:, m], what.rearrange("g p t -> g (p t)")).then_inc(groups_loaded, 16)

            def list_indices(p):
                def body(i):
                    for g in range(2):
                        if not isinstance(i, int):
                            for k in (2 * g, 2 * g + 1):
                                sp.wait_ge(p.rows_ready[k], i * (16 * CHUNK_TILES))
                        sp.dma_start(index[:, g], p.groups[bass.ds(i * 2 + g, 1)].rearrange(
                            "o p t -> (o p) t")).then_inc(p.index_ready[g], 16)
                turns(sp, body)

            def store_table(n):
                sp.wait_ge(table_ready, n)
                sp.dma_start(tabled, hs[:]).then_inc(table_stored, 16)

            sp.wait_ge(row_range_ready, 1)
            with nc.allow_non_contiguous_dma(reason="two ranges a partition"):
                sp.dma_start(range_rows.rearrange("m (p k) -> p m k", k=2), row_range).then_inc(row_range_stored, 16)
            sp.wait_ge(row_range_stored, 16)
            sp.dma_start(ranges, range_rows.unsqueeze(0).to_broadcast([BLOCKS, 2, CHUNKS])).then_inc(ranges_loaded, 16)
            store_table(1)
            sp.wait_ge(rel_index_ready, 1)
            sp.dma_start(rel_groups.rearrange("g p t -> g (p t)"), rel_index[:, 2]).then_inc(rel_index_stored, 16)

            def conv_body(i):
                for g in range(2):
                    if not isinstance(i, int):
                        for k in (2 * g, 2 * g + 1):
                            sp.wait_ge(conv.rows_ready[k], i * (16 * CHUNK_TILES))
                    sp.dma_start(index[:, g], src_groups[bass.ds(i * 2 + g, 1)].rearrange(
                        "o p t -> (o p) t")).then_inc(conv.index_ready[g], 16)
                    for k in (2 * g, 2 * g + 1):
                        wait_from(sp, hidden_psum, i * SLOTS + (k - 1))
                        sp.dma_start(feat_in[:, k % 2], edge_feat[:, bass.ds(
                            i * (SLOTS * CHUNK_EDGES) + k * CHUNK_EDGES, CHUNK_EDGES)]).then_inc(feat_loaded[k % 2], 16)
            turns(sp, conv_body)
            for h in range(HOPS):
                store_table(2 + h)
                list_indices(hops[h])
            store_table(2 + HOPS)
            sp.dma_start(lane_src, src_tiles).then_inc(lane_loaded, 16)
            list_indices(lap)
            sp.wait_ge(lap_out, 1)
            sp.dma_start(lap_rows[0:LAP_GROUPS * LANES].rearrange(
                "(c p l) f -> p c (l f)", p=GROUP_P, l=LANES),
                lap_nodes.rearrange("p (c w) -> p c w", w=P)).then_inc(lap_stored, 16)
            sp.wait_ge(lap_stored, 16)
            full = LAP_GROUPS * LANES // P
            rest = LAP_GROUPS * LANES - full * P
            sp.dma_start(tmp[:, 0:full], lap_rows[0:full * P].rearrange("(b p) f -> p b f", p=P)).then_inc(lap_loaded, 16)
            sp.dma_start(tmp[0:rest, full], lap_rows[full * P:full * P + rest]).then_inc(lap_loaded, 16)
            for n, w in enumerate((rel_w1, rel_w2)):
                if n == 0:
                    sp.wait_ge(lap_out, 2)
                sp.dma_start(rel_w[:, n], w).then_inc(rel_w_loaded, 16)
                for b in range(BLOCKS):
                    sp.wait_ge(rel_copied[b % 2], (BLOCKS + 1 - b % 2) // 2 * n + b // 2 + 1)
                    sp.dma_start(rel_table[b * P * RELS:(b + 1) * P * RELS].rearrange("(p r) c -> p (r c)", r=RELS),
                                 rel_rows[:, b % 2]).then_inc(rel_stored[b % 2], 16)
                if n == 0:
                    sp.wait_ge(rel_index_stored, 16)
                list_indices(rels[n])
                if n == 0:
                    sp.wait_ge(rel_in, 2)
            last = N_NODES // P
            sp.wait_ge(out_ready, 1)
            sp.dma_start(out[0:last * P].rearrange("(b p) f -> p b f", p=P), hs[:, 0:last]).then_inc(out_stored, 16)
            sp.dma_start(out[last * P:N_NODES], hs[0:N_NODES - last * P, last]).then_inc(out_stored, 16)
            sp.wait_ge(out_stored, 32)

        @block.gpsimd
        def _(pool):
            pool.iota(diag[:], [[1, P]], base=0, channel_multiplier=-1, allow_small_or_imprecise_dtypes=True).then_inc(iota_done, 1)
            pool.iota(block_start[:], [[0, 1]], base=0, channel_multiplier=P, allow_small_or_imprecise_dtypes=True).then_inc(iota_done, 1)
            pool.iota(node_iota[:], [[1, NODES]], base=0, channel_multiplier=0, allow_small_or_imprecise_dtypes=True).then_inc(iota_done, 1)

            def gather(p, *stored):
                for stored_sem, value in stored:
                    pool.wait_ge(stored_sem, value)

                def body(i):
                    for k in range(SLOTS):
                        if k % 2 == 0:
                            pool.wait_ge(p.index_ready[k // 2], (i + 1) * 16)
                        if not isinstance(i, int):
                            pool.wait_ge(p.msg_ready, i * SLOTS + (k - SLOTS + 1))
                        pool.sem_inc(p.slots_taken, 1)
                        for t in range(CHUNK_TILES):
                            at = (k % 2) * CHUNK_TILES + t
                            pool.indirect_dma_start(
                                gathered[:, k, t, 0:p.row], None, p.table,
                                bass.IndirectOffsetOnAxis(ap=index[:, k // 2, at:at + 1], axis=0),
                            ).then_inc(p.rows_ready[k], 16)
                turns(pool, body)

            gather(conv, (table_stored, 16))
            for h in range(HOPS):
                gather(hops[h], (table_stored, 16 * (2 + h)))
            gather(lap, (table_stored, 16 * (2 + HOPS)))
            for n in range(2):
                gather(rels[n], *((rel_stored[s], 16 * ((BLOCKS + 1 - s) // 2) * (n + 1)) for s in range(2)))

        @block.tensor
        def _(pe):
            def sum_blocks(p, count_edges=False):
                width = FEAT + 1 if count_edges else FEAT

                def open_block(b):
                    pe.matmul(acc_flat[:, bass.ds(b * ACC_STEP, width)], zeros[:], zeros[:, 0:width],
                              start=True, stop=False)

                def step(b, s, chunk):
                    pe.wait_ge(p.msg_ready, chunk + 1)
                    for t in range(CHUNK_TILES):
                        n = p.vector_tiles
                        if t < n:
                            pe.wait_ge(p.vector_hots, s * n + (t + 1))
                        else:
                            pe.wait_ge(p.scalar_hots, s * (CHUNK_TILES - n) + (t - n + 1))
                        mm = pe.matmul(acc_flat[:, bass.ds(b * ACC_STEP, FEAT)], onehot[:, t],
                                       msgs[:, bass.ds(chunk * CHUNK_TILES + t, 1)].rearrange("p o f -> p (o f)"),
                                       start=False, stop=False)
                        if count_edges:
                            mm = pe.matmul(acc_flat[:, bass.ds(b * ACC_STEP + FEAT, 1)], onehot[:, t], ones[:],
                                           start=False, stop=False)
                        mm.then_inc(p.hot_free, 1)

                def close_block(b):
                    pe.matmul(acc_flat[:, bass.ds(b * ACC_STEP, width)], zeros[:], zeros[:, 0:width],
                              start=False, stop=True).then_inc(p.blocks_done, 1)

                each_step(pe, open_block, step, close_block)

            def turn_nodes(round_):
                for b in range(16 * round_, min(16 * round_ + 16, BLOCKS)):
                    at = (b % 16) * P
                    mm = pe.transpose(work_flat[0:FEAT, at:at + P], hs[:, b], ident[:])
                return mm

            pe.wait_ge(consts_done, 1)
            pe.wait_ge(bounds_ready, 1)
            pe.matmul(acc[0:1, 0, 0:BLOCKS], bounds[:, 0:1], ident[0:BLOCKS, 0:BLOCKS], start=True, stop=True)
            pe.matmul(acc[0:1, 1, 0:BLOCKS], bounds[:, 1:2], ident[0:BLOCKS, 0:BLOCKS], start=True, stop=True)
            pe.matmul(acc[0:1, 2, 0:BLOCKS], bounds[:, 1:2], below[0:BLOCKS], start=True, stop=True)\
                .then_inc(bounds_turned, 1)

            pe.wait_ge(table_ready, 1)
            turn_nodes(0).then_inc(h_turned, 1)
            pe.wait_ge(h_turned_copied, 1)
            turn_nodes(1).then_inc(h_turned, 1)
            pe.wait_ge(h_turned_copied, 2)
            pe.wait_ge(params_loaded, 64)
            pe.wait_ge(spans_ready, 1)
            for b in range(BLOCKS):
                mm = pe.matmul(acc_blocks[:, b, 0:FEAT], node_t[0:FEAT, b * P:(b + 1) * P], self_sb[:],
                               start=True, stop=True)
            mm.then_inc(self_done, 1)

            def conv_body(i):
                for k in range(SLOTS):
                    c = i * SLOTS + k
                    pe.wait_ge(feat_loaded[k % 2], i * 32 + (16 * (k // 2) + 16))
                    wait_from(pe, hidden_ready, c - 1)
                    pe.matmul(work[0:MLP_DIM, k % 2], w1_sb[:], feat_in[:, k % 2],
                              start=True, stop=True).then_inc(hidden_psum, 1)
                    pe.wait_ge(hidden_ready, c + 1)
                    wait_from(pe, mix_read, c)
                    for t in range(CHUNK_TILES):
                        mm = pe.matmul(work[:, 2 + t // 2, (t % 2) * 256:(t % 2) * 256 + 256],
                                       hidden[:, k % 2, t * P:(t + 1) * P], w2_sb[:],
                                       start=True, stop=True)
                    mm.then_inc(mix_ready, 1)
            turns(pe, conv_body)
            pe.wait_ge(vec_self_read, 1)
            sum_blocks(conv, count_edges=True)
            for h in range(HOPS):
                pe.wait_ge(table_ready, 2 + h)
                sum_blocks(hops[h])

            pe.wait_ge(table_ready, 2 + HOPS)
            for half in range(2):
                pe.matmul(acc[:, half, 0:LAP_HALF], zeros[:], node_iota[:, 0:LAP_HALF], start=True, stop=False)
            pe.matmul(work[:, 0, 0:BLOCKS], zeros[:], zeros[:, 0:BLOCKS], start=True, stop=False)

            def lap_body(i):
                for k in range(SLOTS):
                    for t in range(CHUNK_TILES):
                        n = i * (SLOTS * CHUNK_TILES) + (k * CHUNK_TILES + t)
                        pe.wait_ge(lap_tile_ready, n + 1)
                        for half in range(2):
                            pe.matmul(acc[:, half, 0:LAP_HALF], lap_lhs[:, k % 2, t],
                                      group_hot[:, t, half * LAP_HALF:(half + 1) * LAP_HALF],
                                      start=False, stop=False)
                        pe.matmul(work[:, 0, 0:BLOCKS], low_hot[:, t], block_hot[:, t],
                                  start=False, stop=False).then_inc(lap_tile_done, 1)
            turns(pe, lap_body)
            for half in range(2):
                pe.matmul(acc[:, half, 0:LAP_HALF], zeros[:], node_iota[:, 0:LAP_HALF], start=False, stop=True)
            pe.matmul(work[:, 0, 0:BLOCKS], zeros[:], zeros[:, 0:BLOCKS], start=False, stop=True).then_inc(lap_summed, 1)
            pe.wait_ge(lap_copied, 1)
            for c in range(GROUP_COLS):
                at = 512 + c * P
                mm = pe.transpose(work_flat[0:GROUP_P, at:at + P], lap_t[:, c * GROUP_P:(c + 1) * GROUP_P], ident[:])
            mm.then_inc(lap_turned, 1)

            for n in range(2):
                pe.wait_ge(rel_in, 1 + 2 * n)
                turn_nodes(0).then_inc(h_turned, 1)
                pe.wait_ge(h_turned_copied, 3 + 2 * n)
                turn_nodes(1).then_inc(h_turned, 1)
                pe.wait_ge(h_turned_copied, 4 + 2 * n)
                pe.wait_ge(rel_w_loaded, 16 * (n + 1))
                for b in range(BLOCKS):
                    s = b % 2
                    before = (BLOCKS + 1 - s) // 2 * n + b // 2
                    if before:
                        pe.wait_ge(rel_copied[s], before)
                    for half in range(2):
                        mm = pe.matmul(work[:, 2 * s + half], node_t[:, b * P:(b + 1) * P],
                                       rel_w[:, n, half * 512:half * 512 + 512], start=True, stop=True)
                    mm.then_inc(rel_psum[s], 1)
                sum_blocks(rels[n])

        def distances(eng, p, s, b, chunk):
            mine = range(p.vector_tiles, CHUNK_TILES)
            for t in mine:
                eng.wait_ge(p.hot_free, s * CHUNK_TILES + (t + 1))
                eng.activation(distance[:, t], node_iota[:, bass.ds(b * P, P)], ACT.Abs,
                               bias=neg_dst[:, bass.ds(chunk * CHUNK_TILES + t, 1)]).then_inc(p.dist_ready, 1)
            for j, t in enumerate(mine):
                eng.wait_ge(p.dist_ready, s * len(mine) + (j + 1))
                eng.activation(onehot[:, t], distance[:, t], ACT.Relu, bias=1.0, scale=-1.0).then_inc(p.scalar_hots, 1)

        @block.scalar
        def _(act):
            def std(n):
                act.wait_ge(var_ready, n)
                act.activation(stat[:, 3], stat[:, 2], ACT.Sqrt).then_inc(std_ready, 1)

            def onehots(p):
                each_step(act, lambda b: None, lambda b, s, chunk: distances(act, p, s, b, chunk), lambda b: None)

            std(1)

            def conv_body(i):
                for k in range(SLOTS):
                    c = i * SLOTS + k
                    act.wait_ge(hidden_psum, c + 1)
                    wait_from(act, mix_ready, c - 1)
                    act.activation(hidden[0:MLP_DIM, k % 2], work[0:MLP_DIM, k % 2], ACT.Relu,
                                   bias=b1_sb[:]).then_inc(hidden_ready, 1)
            act.wait_ge(params_loaded, 64)
            act.wait_ge(consts_done, 1)
            turns(act, conv_body)
            act.wait_ge(spans_ready, 1)
            act.wait_ge(setup_done, 1)
            onehots(conv)
            std(2)
            for h in range(HOPS):
                onehots(hops[h])
            std(3)
            std(4)
            for n in range(2):
                for b in range(1, BLOCKS, 2):
                    act.wait_ge(rel_psum[1], BLOCKS // 2 * n + b // 2 + 1)
                    before = BLOCKS // 2 * n + b // 2
                    if before:
                        act.wait_ge(rel_stored[1], 16 * before)
                    act.activation(rel_rows[:, 1], work_flat[:, 2 * 512:4 * 512], ACT.Copy).then_inc(rel_copied[1], 1)
                onehots(rels[n])
                if n == 0:
                    act.wait_ge(rels[0].blocks_done, BLOCKS)
                    act.activation(hs[:], acc_blocks[:, :, 0:FEAT], ACT.Tanh).then_inc(tanh_done, 1)

        @block.vector
        def _(v):
            done = [0]

            def step(ins):
                done[0] += 1
                ins.then_inc(vec, 1)
                v.wait_ge(vec, done[0])

            def bcast(row):
                return row.unsqueeze(2).to_broadcast([P, BLOCKS, FEAT])

            def norm_relu(n):
                step(v.tensor_reduce(stat[:, 0], xs[:], AX_X, ALU.add))
                step(v.tensor_scalar(stat[:, 0], stat[:, 0], 1.0 / FEAT, None, ALU.mult))
                step(v.tensor_tensor(tmp[:], xs[:], bcast(stat[:, 0]), ALU.subtract))
                step(v.tensor_tensor(hs[:], tmp[:], tmp[:], ALU.mult))
                step(v.tensor_reduce(stat[:, 1], hs[:], AX_X, ALU.add))
                step(v.tensor_scalar(stat[:, 2], stat[:, 1], 1.0 / FEAT, EPS, ALU.mult, ALU.add))
                v.sem_inc(var_ready, 1)
                v.wait_ge(std_ready, n)
                step(v.reciprocal(stat[:, 4], stat[:, 3]))
                step(v.tensor_tensor(tmp[:], tmp[:], bcast(stat[:, 4]), ALU.mult))
                step(v.tensor_scalar(hs[:], tmp[:], 0.0, None, ALU.max))

            def onehots(p):
                def one_step(b, s, chunk):
                    for t in range(p.vector_tiles):
                        v.wait_ge(p.hot_free, s * CHUNK_TILES + (t + 1))
                        v.tensor_scalar(onehot[:, t], node_iota[:, bass.ds(b * P, P)],
                                        neg_dst[:, bass.ds(chunk * CHUNK_TILES + t, 1)], 0.0,
                                        ALU.add, ALU.is_equal).then_inc(p.vector_hots, 1)
                each_step(v, lambda b: None, one_step, lambda b: None)

            def free_onehots(p):
                v.sem_inc(p.hot_free, CHUNK_TILES * (CHUNKS + 1))
                if p.vector_tiles:
                    v.sem_inc(p.vector_hots, p.vector_tiles * CHUNKS)
                v.sem_inc(p.scalar_hots, (CHUNK_TILES - p.vector_tiles) * CHUNKS)
                v.sem_inc(p.dist_ready, (CHUNK_TILES - p.vector_tiles) * CHUNKS)

            def turn_copies(first):
                for r in range(2):
                    v.wait_ge(h_turned, first + r)
                    n = min(16, BLOCKS - 16 * r) * P
                    step(v.tensor_copy(node_t[0:FEAT, 16 * P * r:16 * P * r + n], work_flat[0:FEAT, 0:n]))
                    v.sem_inc(h_turned_copied, 1)

            v.wait_ge(iota_done, 3)
            v.tensor_scalar(ident[:], diag[:], 0.0, None, ALU.is_equal)
            v.tensor_scalar(below[:], diag[:, 0:BLOCKS], 0.0, None, ALU.is_gt)
            v.memset(zeros[:], 0.0)
            v.memset(hidden[MLP_DIM:MLP_DIM + 1], 1.0)
            step(v.memset(ones[:], 1.0))
            v.sem_inc(consts_done, 1)

            v.wait_ge(x_loaded, 16)
            norm_relu(1)
            v.sem_inc(table_ready, 1)

            v.wait_ge(rows_loaded, 16)
            rows = setup_rows.rearrange("p (k e) -> p k e", k=2)
            v.tensor_reduce(row_range[:, 0], rows, AX_X, ALU.min)
            step(v.tensor_reduce(row_range[:, 1], rows, AX_X, ALU.max))
            v.sem_inc(row_range_ready, 1)
            v.wait_ge(ranges_loaded, 16)
            low, high, inside = range_tmp[:, 0], range_tmp[:, 1], range_tmp[:, 2]
            start = block_start[0:BLOCKS]
            step(v.tensor_scalar(bounds[:, 2:3], start, float(P - 1), None, ALU.add))
            step(v.tensor_scalar(low, ranges[:, 0], bounds[:, 2:3], None, ALU.is_le))
            step(v.tensor_scalar(high, ranges[:, 1], start, None, ALU.is_ge))
            step(v.tensor_tensor(inside, low, high, ALU.mult))
            chunk_no = node_iota[0:BLOCKS, 0:CHUNKS]
            step(v.tensor_scalar(low, chunk_no, float(-(CHUNKS - 1)), None, ALU.add))
            step(v.tensor_tensor(low, low, inside, ALU.mult))
            step(v.tensor_reduce(bounds[:, 3:4], low, AX_X, ALU.min))
            step(v.tensor_scalar(bounds[:, 0:1], bounds[:, 3:4], float(CHUNKS - 1), None, ALU.add))
            step(v.tensor_scalar(high, chunk_no, 1.0, None, ALU.add))
            step(v.tensor_tensor(high, high, inside, ALU.mult))
            step(v.tensor_reduce(bounds[:, 4:5], high, AX_X, ALU.max))
            step(v.tensor_tensor(bounds[:, 5:6], bounds[:, 4:5], bounds[:, 0:1], ALU.subtract))
            step(v.tensor_scalar(bounds[:, 1:2], bounds[:, 5:6], 1.0, None, ALU.max))
            v.sem_inc(bounds_ready, 1)
            v.wait_ge(bounds_turned, 1)
            step(v.tensor_copy(span_rows[:], acc[0:1, 0:3, 0:BLOCKS]))
            step(v.tensor_tensor(span_rows[:, 1], span_rows[:, 1], span_rows[:, 0], ALU.add))
            step(v.tensor_tensor(span_rows[:, 2], span_rows[:, 2], span_rows[:, 0], ALU.subtract))
            step(v.tensor_scalar(span_rows[:, 2], span_rows[:, 2], float(CHUNKS), None, ALU.add))
            step(v.tensor_copy(spans[:].rearrange("p (m b) -> p m b", m=3)[:, :, 0:BLOCKS], span_rows[:]))
            v.sem_inc(spans_ready, 1)

            turn_copies(1)
            v.wait_ge(self_done, 1)
            step(v.scalar_tensor_tensor(out=xs[:], in0=acc_blocks[:, :, 0:FEAT], scalar=float(SI_SCALE), in1=xs[:],
                                        op0=ALU.mult, op1=ALU.add))
            v.sem_inc(vec_self_read, 1)

            v.wait_ge(tiles_loaded, 64)
            v.tensor_scalar(neg_dst[:], setup_dst, -1.0, None, ALU.mult)
            step(v.tensor_scalar(setup_tmp, setup_src, 2, None, ALU.logical_shift_right))
            step(v.tensor_copy(src_group[:], setup_tmp))
            step(v.tensor_scalar(setup_tmp, setup_src, 7, None, ALU.logical_shift_right))
            step(v.tensor_copy(src_block[:], setup_tmp))
            step(v.tensor_scalar(setup_tmp, setup_src, P - 1, None, ALU.bitwise_and))
            step(v.tensor_copy(src_low[:], setup_tmp))
            v.wait_ge(groups_loaded, 32)
            step(v.scalar_tensor_tensor(out=rel_index[:, 2], in0=rel_index[:, 0], scalar=float(RELS),
                                        in1=rel_index[:, 1], op0=ALU.mult, op1=ALU.add))
            v.sem_inc(rel_index_ready, 1)
            v.wait_ge(rel_index_stored, 16)
            v.sem_inc(setup_done, 1)
            free_onehots(conv)

            def conv_body(i):
                for k in range(SLOTS):
                    c = i * SLOTS + k
                    base = i * (6 * SLOTS) + 6 * k
                    tiles = bass.ds(i * (SLOTS * CHUNK_TILES) + k * CHUNK_TILES, CHUNK_TILES)
                    shape3 = [P, CHUNK_TILES, MUL]
                    g_s = gathered[:, k, :, 0:MUL]
                    g_v = gathered[:, k, :, MUL:FEAT].rearrange("p t (i m) -> p t i m", m=3)
                    v.tensor_scalar(scaled_sh[:, :, 0:4], sh[:, tiles], ALPHA, None, ALU.mult)
                    v.tensor_scalar(scaled_sh[:, :, 4:7], sh[:, tiles, 1:4], float(ALPHA * C110), None,
                                    ALU.mult).then_inc(conv_step, 1)
                    v.wait_ge(conv.rows_ready[k], (i + 1) * (16 * CHUNK_TILES))
                    v.wait_ge(conv_step, base + 1)
                    v.tensor_tensor(dots[:], g_v, scaled_sh[:, :, 4:7].unsqueeze(2).to_broadcast(
                        [P, CHUNK_TILES, MUL, 3]), ALU.mult).then_inc(conv_step, 1)
                    v.tensor_tensor(coef[:, :, 0], g_s, scaled_sh[:, :, 0:1].to_broadcast(shape3), ALU.mult)
                    v.tensor_copy(coef[:, :, 2], g_s)
                    v.tensor_tensor(coef[:, :, 3:6].rearrange("p t m i -> p t i m"), g_v,
                                    scaled_sh[:, :, 0:1].unsqueeze(3).to_broadcast([P, CHUNK_TILES, MUL, 3]), ALU.mult)
                    v.wait_ge(conv_step, base + 2)
                    v.tensor_reduce(coef[:, :, 1], dots[:], AX_X, ALU.add).then_inc(conv_step, 1)
                    v.wait_ge(mix_ready, c + 1)
                    v.wait_ge(conv_step, base + 3)
                    mix = work_flat[:, 1024:2048].rearrange("p (t c) -> p t c", t=CHUNK_TILES)
                    v.tensor_tensor(
                        prods[:, :, 0:4].rearrange("p t n i o -> p t (n i) o"),
                        mix.rearrange("p t (n o) -> p t n o", o=MUL),
                        coef[:, :, 0:4].rearrange("p t n i -> p t (n i)").unsqueeze(3).to_broadcast(
                            [P, CHUNK_TILES, 4 * MUL, MUL]), ALU.mult)
                    for m in (4, 5):
                        ins = v.tensor_tensor(
                            prods[:, :, m], mix[:, :, 192:256].rearrange("p t (i o) -> p t i o", o=MUL),
                            coef[:, :, m].unsqueeze(3).to_broadcast([P, CHUNK_TILES, MUL, MUL]), ALU.mult)
                    ins.then_inc(mix_read, 1)
                    v.wait_ge(mix_read, c + 1)
                    v.tensor_reduce(
                        sums[:].rearrange("p t n o -> p (t n) o"),
                        prods[:].rearrange("p t n i o -> p (t n) o i"), AX_X, ALU.add).then_inc(conv_step, 1)
                    v.wait_ge(conv_step, base + 4)
                    v.tensor_tensor(msgs[:, tiles, 0:MUL], sums[:, :, 0], sums[:, :, 1], ALU.add)
                    v.tensor_tensor(spread[:], sums[:, :, 2].unsqueeze(3).to_broadcast([P, CHUNK_TILES, MUL, 3]),
                                    scaled_sh[:, :, 1:4].unsqueeze(2).to_broadcast([P, CHUNK_TILES, MUL, 3]),
                                    ALU.mult).then_inc(conv_step, 1)
                    v.wait_ge(conv_step, base + 5)
                    v.tensor_tensor(msgs[:, tiles, MUL:FEAT].rearrange("p t (o m) -> p t o m", m=3), spread[:],
                                    sums[:, :, 3:6].rearrange("p t m o -> p t o m"), ALU.add).then_inc(conv_step, 1)
                    v.wait_ge(conv_step, base + 6)
                    v.sem_inc(conv.msg_ready, 1)
            turns(v, conv_body)
            onehots(conv)
            v.wait_ge(conv.blocks_done, BLOCKS)
            step(v.tensor_copy(mean_scale[:], acc_blocks[:, :, FEAT]))
            step(v.tensor_scalar(mean_scale[:], mean_scale[:], 1.0, None, ALU.max))
            step(v.reciprocal(mean_scale[:], mean_scale[:]))
            step(v.tensor_tensor(xs[:], xs[:], acc_blocks[:, :, 0:FEAT], ALU.add))

            norm_relu(2)
            step(v.tensor_scalar(final[:], hs[:], 1.0 / (HOPS + 1), None, ALU.mult))
            for h, p in enumerate(hops):
                free_onehots(p)
                v.sem_inc(table_ready, 1)

                def hop_body(i):
                    for k in range(SLOTS):
                        v.wait_ge(p.rows_ready[k], (i + 1) * (16 * CHUNK_TILES))
                        v.tensor_copy(msgs[:, bass.ds(i * (SLOTS * CHUNK_TILES) + k * CHUNK_TILES, CHUNK_TILES)],
                                      gathered[:, k, :, 0:FEAT]).then_inc(p.msg_ready, 1)
                turns(v, hop_body)
                v.wait_ge(p.blocks_done, BLOCKS)
                step(v.tensor_tensor(hs[:], acc_blocks[:, :, 0:FEAT], bcast(mean_scale[:]), ALU.mult))
                step(v.scalar_tensor_tensor(out=final[:], in0=hs[:], scalar=1.0 / (HOPS + 1), in1=final[:],
                                            op0=ALU.mult, op1=ALU.add))
            step(v.tensor_tensor(xs[:], xs[:], final[:], ALU.add))

            norm_relu(3)
            v.sem_inc(table_ready, 1)
            v.wait_ge(lane_loaded, 16)
            step(v.tensor_scalar(lane_tmp, lane_src, LANES - 1, None, ALU.bitwise_and))
            step(v.tensor_copy(lane, lane_tmp))
            for n in range(LANES):
                step(v.scalar_tensor_tensor(out=lane_weight[:, :, n], in0=lane, scalar=float(n), in1=weight[:],
                                            op0=ALU.is_equal, op1=ALU.mult))

            def lap_body(i):
                for k in range(SLOTS):
                    v.wait_ge(lap.rows_ready[k], (i + 1) * (16 * CHUNK_TILES))
                    wait_from(v, lap_tile_done, i * (SLOTS * CHUNK_TILES) + (k - 1) * CHUNK_TILES)
                    v.tensor_tensor(
                        lap_lhs[:, k % 2].rearrange("p t (l f) -> p t l f", l=LANES),
                        gathered[:, k, :, 0:FEAT].unsqueeze(2).to_broadcast([P, CHUNK_TILES, LANES, FEAT]),
                        lane_weight[:, bass.ds(i * (SLOTS * CHUNK_TILES) + k * CHUNK_TILES, CHUNK_TILES)].unsqueeze(3)
                        .to_broadcast([P, CHUNK_TILES, LANES, FEAT]), ALU.mult).then_inc(lap.msg_ready, 1)
                    for t in range(CHUNK_TILES):
                        n = i * (SLOTS * CHUNK_TILES) + (k * CHUNK_TILES + t)
                        col = bass.ds(n, 1)
                        wait_from(v, lap_tile_done, i * (SLOTS * CHUNK_TILES) + (k * CHUNK_TILES + t - 3))
                        v.tensor_scalar(low_hot[:, t], node_iota[:, 0:P], src_low[:, col], None, ALU.is_equal)
                        v.tensor_scalar(block_hot[:, t], node_iota[:, 0:BLOCKS], src_block[:, col],
                                        weight[:, col], ALU.is_equal, ALU.mult)
                        v.tensor_scalar(group_hot[:, t], node_iota[:, 0:LAP_GROUPS], src_group[:, col], None,
                                        ALU.is_equal).then_inc(lap_tile_ready, 1)
            turns(v, lap_body)
            v.wait_ge(lap_summed, 1)
            v.tensor_copy(lap_t[:, 0:LAP_HALF], acc[:, 0, 0:LAP_HALF])
            step(v.tensor_copy(lap_t[:, LAP_HALF:LAP_GROUPS], acc[:, 1, 0:LAP_HALF]))
            v.sem_inc(lap_copied, 1)
            step(v.tensor_copy(out_weight[:], work[:, 0, 0:BLOCKS]))
            v.wait_ge(lap_turned, 1)
            step(v.tensor_copy(lap_nodes, work_flat[0:GROUP_P, 512:512 + GROUP_COLS * P]))
            step(v.memset(tmp[:, BLOCKS - 1], 0.0))
            v.sem_inc(lap_out, 1)
            step(v.tensor_tensor(hs[:], hs[:], bcast(out_weight[:]), ALU.mult))
            step(v.tensor_tensor(xs[:], xs[:], hs[:], ALU.subtract))
            v.wait_ge(lap_loaded, 32)
            v.sem_inc(lap_out, 1)
            step(v.tensor_tensor(xs[:], xs[:], tmp[:], ALU.add))
            norm_relu(4)

            for n, p in enumerate(rels):
                v.sem_inc(rel_in, 1)
                free_onehots(p)
                step(v.memset(node_t[FEAT:FEAT + 1], 1.0))
                turn_copies(3 + 2 * n)
                for b in range(0, BLOCKS, 2):
                    before = (BLOCKS + 1) // 2 * n + b // 2
                    v.wait_ge(rel_psum[0], before + 1)
                    if before:
                        v.wait_ge(rel_stored[0], 16 * before)
                    v.tensor_copy(rel_rows[:, 0], work_flat[:, 0:2 * 512]).then_inc(rel_copied[0], 1)
                for s in range(2):
                    v.wait_ge(rel_stored[s], 16 * ((BLOCKS + 1 - s) // 2) * (n + 1))

                def rel_body(i):
                    for k in range(SLOTS):
                        tiles = bass.ds(i * (SLOTS * CHUNK_TILES) + k * CHUNK_TILES, CHUNK_TILES)
                        rows4 = gathered[:, k].rearrange("p t (q o) -> p t q o", q=Q)
                        v.wait_ge(p.rows_ready[k], (i + 1) * (16 * CHUNK_TILES))
                        v.tensor_tensor(rows4, rows4, sh[:, tiles].unsqueeze(3).to_broadcast(
                            [P, CHUNK_TILES, Q, FEAT]), ALU.mult).then_inc(rel_prod[n], 1)
                        v.wait_ge(rel_prod[n], i * SLOTS + (k + 1))
                        v.tensor_reduce(msgs[:, tiles], rows4.rearrange("p t q o -> p t o q"), AX_X,
                                        ALU.add).then_inc(p.msg_ready, 1)
                turns(v, rel_body)
                if n == 0:
                    v.wait_ge(tanh_done, 1)
                    v.sem_inc(rel_in, 1)
                else:
                    v.wait_ge(p.blocks_done, BLOCKS)
                    step(v.tensor_tensor(hs[:], acc_blocks[:, :, 0:FEAT], xs[:], ALU.add))
                    v.sem_inc(out_ready, 1)


_INS = ["x", "dst_rows", "src_groups", "dst_groups", "type_groups", "src_tiles", "dst_tiles", "weight_tiles",
        "sh_tiles", "edge_feat", "w1", "b1", "w2", "self_w", "rel_w1", "rel_w2"]


def _lay_out(x, src, dst, edge_attr_32, edge_attr_4, edge_type_8, edge_weight, L0_gnn_W1, L0_gnn_b1, L0_gnn_W2,
             L0_gnn_b2, L0_gnn_si_w0, L0_gnn_si_w1, L3_gnn_W1, L3_gnn_b1, L3_gnn_W2, L3_gnn_b2):
    a = np.asarray

    def padded(v, rows, fill=0):
        v = a(v)
        return np.concatenate([v, np.full((rows - v.shape[0],) + v.shape[1:], fill, v.dtype)])

    def tiles(v):
        v = v.reshape((TILES, P) + v.shape[1:])
        return np.ascontiguousarray(v.swapaxes(0, 1))

    def groups(v):
        return np.ascontiguousarray(v.reshape(GROUPS, GROUP_TILES, P).swapaxes(1, 2))

    s, d = padded(src, EDGES, PAD_NODE), padded(dst, EDGES, PAD_NODE)
    order = [0, 3, 1, 2]
    w2 = np.concatenate([a(L0_gnn_W2), a(L0_gnn_b2)[None]]).reshape(MLP_DIM + 1, PATHS, MUL * MUL)[:, order]
    self_w = np.zeros((FEAT, FEAT), a(L0_gnn_si_w0).dtype)
    self_w[:MUL, :MUL] = a(L0_gnn_si_w0)
    for m in range(3):
        self_w[MUL + m::3, MUL + m::3] = a(L0_gnn_si_w1)

    def rel(w, b):
        return np.concatenate([a(w).transpose(2, 0, 1, 3).reshape(FEAT, -1), a(b).reshape(1, -1)])

    return dict(
        x=padded(x, NODES), dst_rows=d.reshape(CHUNKS, CHUNK_EDGES), src_groups=groups(s), dst_groups=groups(d),
        type_groups=groups(padded(edge_type_8, EDGES)), src_tiles=tiles(s), dst_tiles=tiles(d),
        weight_tiles=tiles(padded(edge_weight, EDGES)), sh_tiles=tiles(padded(edge_attr_4, EDGES)),
        edge_feat=np.ascontiguousarray(padded(edge_attr_32, EDGES).T), w1=a(L0_gnn_W1), b1=a(L0_gnn_b1)[:, None],
        w2=np.ascontiguousarray(w2.reshape(MLP_DIM + 1, -1)), self_w=self_w,
        rel_w1=rel(L3_gnn_W1, L3_gnn_b1), rel_w2=rel(L3_gnn_W2, L3_gnn_b2))


def kernel(**inputs):
    import concourse.bacc as bacc
    from concourse.bass_utils import run_bass_kernel_spmd

    nc = bacc.Bacc("TRN2", target_bir_lowering=False, num_devices=1)
    laid = _lay_out(**inputs)
    args, arrays = [], {}
    for name in _INS:
        arr = np.ascontiguousarray(laid[name])
        arrays[f"in_{name}"] = arr
        args.append(nc.dram_tensor(f"in_{name}", arr.shape, mybir.dt.from_np(arr.dtype), kind="ExternalInput").ap())
    args.append(nc.dram_tensor("out_x", (N_NODES, FEAT), F32, kind="ExternalOutput").ap())
    build(nc, *args)
    result = run_bass_kernel_spmd(nc, [arrays], core_ids=[0])
    return result.results[0]["out_x"]
```
